# Optimizing a Trainium2 kernel written in Bass

```python
import numpy as np
import jax
import jax.numpy as jnp

def _softmax(x, axis=-1):
    return jax.nn.softmax(x, axis=axis)

def _gelu(x):
    return jax.nn.gelu(x, approximate=True)

def _silu(x):
    return jax.nn.silu(x)

def _sigmoid(x):
    return jax.nn.sigmoid(x)

def _layernorm(x, axis=-1, eps=1e-05):
    m = jnp.mean(x, axis=axis, keepdims=True)
    v = jnp.var(x, axis=axis, keepdims=True)
    return (x - m) / jnp.sqrt(v + eps)

def _scatter_add(tgt, idx, src, axis=0):
    return tgt.at[idx].add(src)

def _segment_sum(src, seg, n):
    return jax.ops.segment_sum(src, seg, n)
kernel_name = 'mk_cond_seq_d1_seqx_r2_5e6902'

def setup_inputs(seed: int=0):
    np.random.seed(seed)
    _w = jnp.asarray

    def _rec_inputs():
        import jax
        import jax.numpy as jnp
        _rk = jax.random.key(seed)
        x = -0.0003929 + 0.9999 * jax.random.normal(jax.random.fold_in(_rk, 1), (64, 128, 512), jnp.float32)
        _lenS = 128 - jax.random.randint(jax.random.fold_in(_rk, 7), (64,), 0, max(1, 128 // 4) + 1, jnp.int32)
        _lenS2 = 128 - jax.random.randint(jax.random.fold_in(_rk, 8), (64,), 0, max(1, 128 // 4) + 1, jnp.int32)
        cond_256 = -0.0209273 + 1.04763 * jax.random.normal(jax.random.fold_in(_rk, 11), (64, 128), jnp.float32)
        return (x, cond_256)
    x, cond_256 = _rec_inputs()

    def _L0_cond_setup():
        import jax, jax.numpy as jnp
        import numpy as np
        EPS = 1e-06

        def act_quant(x):
            scale = 127.0 / jnp.clip(jnp.max(jnp.abs(x), axis=-1, keepdims=True), 1e-05, None)
            return jnp.clip(jnp.round(x * scale), -128.0, 127.0) / scale

        def weight_quant(w):
            scale = 1.0 / jnp.clip(jnp.mean(jnp.abs(w)), 1e-05, None)
            return jnp.clip(jnp.round(w * scale), -1.0, 1.0) / scale
        key = jax.random.key(seed)
        k0, k1, k2, k3, k4 = jax.random.split(key, 5)
        B, S, D, FF, C = (4, 2048, 512, 2048, 128)
        return {'x': jax.random.normal(k0, (B, S, D), jnp.float32), 'cond': jax.random.normal(k1, (B, C), jnp.float32), 'norm_w': jax.random.normal(k2, (D, C), jnp.float32) * 0.02, 'up_w': jax.random.normal(k3, (2 * FF, D), jnp.float32) * 0.02, 'down_w': jax.random.normal(k4, (D, FF), jnp.float32) * 0.02}
    _L0_cond_all = _L0_cond_setup()
    _L0_cond_in = {k: v for k, v in _L0_cond_all.items() if k in ('norm_w', 'up_w', 'down_w')}
    del _L0_cond_all
    return {'x': x, 'cond_256': cond_256, 'L0_cond_norm_w': _L0_cond_in['norm_w'], 'L0_cond_up_w': _L0_cond_in['up_w'], 'L0_cond_down_w': _L0_cond_in['down_w']}

def reference(x, cond_256, L0_cond_norm_w, L0_cond_up_w, L0_cond_down_w):
    import jax
    import jax.numpy as jnp

    def _L0_cond_ref(x, cond, norm_w, up_w, down_w):
        import jax, jax.numpy as jnp
        import numpy as np
        EPS = 1e-06

        def act_quant(x):
            scale = 127.0 / jnp.clip(jnp.max(jnp.abs(x), axis=-1, keepdims=True), 1e-05, None)
            return jnp.clip(jnp.round(x * scale), -128.0, 127.0) / scale

        def weight_quant(w):
            scale = 1.0 / jnp.clip(jnp.mean(jnp.abs(w)), 1e-05, None)
            return jnp.clip(jnp.round(w * scale), -1.0, 1.0) / scale
        scale = cond @ norm_w.T + 1.0
        ms = jnp.mean(x * x, axis=-1, keepdims=True)
        h = x * (scale[:, None, :] * jax.lax.rsqrt(ms + EPS))
        u = h @ up_w.T
        val, gate = jnp.split(u, 2, axis=-1)
        h = val * jax.nn.gelu(gate, approximate=False)
        hq = h + jax.lax.stop_gradient(act_quant(h) - h)
        wq = down_w + jax.lax.stop_gradient(weight_quant(down_w) - down_w)
        y = hq @ wq.T
        return y + x
    x = _L0_cond_ref(x, cond_256, L0_cond_norm_w, L0_cond_up_w, L0_cond_down_w)
    return x

_drawn_inputs = setup_inputs


def setup_inputs(seed=0):
    import zlib

    import numpy as np

    out = dict(_drawn_inputs(seed))
    spreads = {}
    factors = {}
    for name, (base, spread) in spreads.items():
        noise = np.random.default_rng([zlib.crc32(name.encode()), seed]).standard_normal(out[name].shape)
        drawn = base * np.exp(spread * noise) if base else spread * noise
        out[name] = jnp.asarray(drawn.astype(out[name].dtype))
    for name, factor in factors.items():
        out[name] = (out[name] * factor).astype(out[name].dtype)
    return out
```

```python
from contextlib import ExitStack

import concourse.bass as bass
from concourse import mybir

F32 = mybir.dt.float32
F16 = mybir.dt.float16
BF16 = mybir.dt.bfloat16
I32 = mybir.dt.int32
ALU = mybir.AluOpType
ACT = mybir.ActivationFunctionType
AX_X = mybir.AxisListType.X
ABSMAX = bass.bass_isa.ReduceOp.absmax

P = 128
EPS = 1e-6
CLIP = 1e-5
QMAX = 127.0
ROUND = 12582912.0
EXPONENT = 0x7F800000
W_UP = 2.0 ** 12
H_UP = 2.0 ** 9
UNDO_W = 2.0 ** -13
UNDO_H = 2.0 ** -10
TINY = 1e-30


def bass_bitlinear_glu_kernel(
    nc: bass.Bass,
    x: bass.AP,
    cond: bass.AP,
    norm_w: bass.AP,
    up_w: bass.AP,
    down_w: bass.AP,
    out: bass.AP,
):
    NBATCH, T, D = x.shape
    C = cond.shape[1]
    FF = down_w.shape[1]
    KD = D // P
    NF = FF // P
    TG = 4
    NT = TG * P
    G = NBATCH // TG
    U = 4
    NI = NF // U
    assert T == P and C == P and NI == TG and NT == 512 and D == 512
    WT = 2 * KD * 2 * P
    XG = TG * D
    HP = KD * NT
    XSLOTS = 4

    x_g = x.rearrange("(g b) t d -> g t b d", b=TG)
    out_b = out
    upw_c = up_w.rearrange("(h c j p) d -> h c p j d", h=2, j=2, p=P)
    downw_t = down_w.rearrange("(t p) f -> t p f", p=P)

    with ExitStack() as ctx:
        def sb(name, shape, dt):
            return ctx.enter_context(nc.sbuf_tensor(name, shape, dt))

        def sem(name):
            return ctx.enter_context(nc.semaphore(name))

        wT = sb("wT", [P, NF * WT], F16)
        tern_q = sb("tern_q", [P, NF * (D + NT)], BF16)
        tern = tern_q[:, 0:NF * D]
        q = tern_q[:, NF * D:]
        h = sb("h", [P, NF * NT], F32)
        xbuf = sb("xbuf", [P, XSLOTS * XG], F32)
        hT = sb("hT", [P, 2 * 2 * HP], F16)
        xn = sb("xn", [P, D], F32)
        hs = sb("hs", [P, KD, P], F32)
        glu = sb("glu", [P, 2, NT], F32)
        runmax = sb("runmax", [P, NT], F32)
        scaleT = sb("scaleT", [P, NBATCH, KD], F32)
        ident = sb("ident", [P, P], F32)
        identb = sb("identb", [P, P], BF16)
        ones = sb("ones", [P, P], F32)
        unscale = sb("unscale", [P, NF, 2], F32)
        wmax = sb("wmax", [P, 2], F32)
        wpow = sb("wpow", [P, 2], F32)
        winv = sb("winv", [P, 4, 2], F32)
        ssq = sb("ssq", [P, 1], F32)
        msq = sb("msq", [P, 1], F32)
        rstd = sb("rstd", [P, 1], F32)
        rms_consts = sb("rms_consts", [P, 3], F32)
        smax = sb("smax", [P, 1], F32)
        smax_all = sb("smax_all", [P, 1], F32)
        spow = sb("spow", [P, 1], F32)
        sinv = sb("sinv", [P, 1], F32)
        sundo = sb("sundo", [P, 1], F32)
        mtok = sb("mtok", [P, TG], F32)
        minv = sb("minv", [P, TG], F32)
        stok = sb("stok", [P, TG], F32)
        ctok = sb("ctok", [P, TG], F32)
        asum = sb("asum", [P, KD], F32)
        asum1 = sb("asum1", [P, 1], F32)
        wmean = sb("wmean", [P, 1], F32)
        wrecip = sb("wrecip", [P, 1], F32)
        wmean127 = sb("wmean127", [P, 1], F32)

        banks = ctx.enter_context(nc.psum_tensor("banks", [P, 8, 512], F32))
        gate_ps = [banks[:, 0, :], banks[:, 1, :]]
        val_ps = [banks[:, 2, :], banks[:, 3, :]]
        last_ps = gate_ps + val_ps
        down_ps = [banks[:, 4, :], banks[:, 5, :]]
        xT_ps = banks[:, 6, :]
        stat_ps = banks[:, 7, :]

        stage = xbuf[:, 2 * XG:4 * XG].rearrange("p (s h j d) -> p s h j d", s=2, h=2, j=2)
        vb = xbuf[:, 2 * XG:4 * XG].bitcast(BF16).rearrange("p (t f) -> p t f", t=KD)
        raw_flat = tern_q[:, :].bitcast(F32)
        nw = h[:, 0:KD * P].rearrange("p (k c) -> p k c", k=KD)
        cnd = h[0:NBATCH, 512:512 + P]
        nwT = h[:, 1024:1024 + D]
        cndT = h[:, 1536:1536 + NBATCH]

        x_loaded = sem("x_loaded")
        nw_loaded = sem("nw_loaded")
        stage_loaded = [sem("stage_loaded0"), sem("stage_loaded1")]
        raw_loaded = sem("raw_loaded")
        consts_zero = sem("consts_zero")
        consts_ready = sem("consts_ready")
        identb_ready = sem("identb_ready")
        nwT_ready = sem("nwT_ready")
        nwT_copied = sem("nwT_copied")
        scale_mm = sem("scale_mm")
        scale_one = sem("scale_one")
        smax_ready = sem("smax_ready")
        smax_reduced = sem("smax_reduced")
        spow_ready = sem("spow_ready")
        scale_ready = sem("scale_ready")
        ssq_ready = sem("ssq_ready")
        msq_ready = sem("msq_ready")
        rstd_ready = sem("rstd_ready")
        xn_ready = sem("xn_ready")
        xT_ready = sem("xT_ready")
        hs_ready = sem("hs_ready")
        hi_ready = sem("hi_ready")
        lo_ready = sem("lo_ready")
        wmax_ready = sem("wmax_ready")
        wclamped = sem("wclamped")
        wpow_ready = sem("wpow_ready")
        wcomplement = sem("wcomplement")
        winv_ready = sem("winv_ready")
        unscale_ready = sem("unscale_ready")
        wscaled = sem("wscaled")
        wT_ready = sem("wT_ready")
        whi_ready = sem("whi_ready")
        wlo_ready = sem("wlo_ready")
        asum_ready = sem("asum_ready")
        asum1_ready = sem("asum1_ready")
        wsum_ready = sem("wsum_ready")
        wmean_ready = sem("wmean_ready")
        wrecip_ready = sem("wrecip_ready")
        raw_magic = sem("raw_magic")
        vb_ready = sem("vb_ready")
        ternT_ready = sem("ternT_ready")
        tern_ready = sem("tern_ready")
        gate_ready = sem("gate_ready")
        val_ready = sem("val_ready")
        gelu_ready = sem("gelu_ready")
        h_ready = sem("h_ready")
        abs_ready = sem("abs_ready")
        runmax_zero = sem("runmax_zero")
        max_ready = sem("max_ready")
        maxT_ready = sem("maxT_ready")
        mraw_ready = sem("mraw_ready")
        mtok_ready = sem("mtok_ready")
        minv_ready = sem("minv_ready")
        stok_ready = sem("stok_ready")
        ctok_ready = sem("ctok_ready")
        sbc_ready = sem("sbc_ready")
        hscaled = sem("hscaled")
        q_ready = sem("q_ready")
        down_ready = sem("down_ready")
        y_ready = sem("y_ready")
        stored = sem("stored")

        def weight(j, half, k, part):
            return wT[:, bass.ds(j * WT + ((half * KD + k) * 2 + part) * P, P)]

        def const_col(c):
            return rms_consts[:, c:c + 1]

        def x_tile(slot, i):
            return xbuf[:, bass.ds(slot * XG + i * D, D)]

        def raw(t):
            return raw_flat[:, bass.ds(t * FF, FF)]

        def tile_of(buf, j):
            return buf[:, bass.ds(j * NT, NT)]

        block = ctx.enter_context(nc.Block())

        @block.sync
        def _(sp):
            def load_x(g, slot):
                sp.dma_start(xbuf[:, bass.ds(slot * XG, XG)].rearrange("p (b d) -> p b d", b=TG),
                             x_g[g]).then_inc(x_loaded, 16)

            def load_stage(c, s):
                for half in range(2):
                    sp.dma_start(stage[:, s, half], upw_c[half, c]).then_inc(stage_loaded[s], 16)

            def load_raw(t):
                sp.dma_start(raw(t), downw_t[t]).then_inc(raw_loaded, 16)

            def store_group(g, slot, first):
                for i in range(TG):
                    sp.wait_ge(y_ready, first + i + 1)
                    sp.dma_start(out_b[g * TG + i], x_tile(slot, i)).then_inc(stored, 16)

            sp.dma_start(nw, norm_w.rearrange("(k p) c -> p k c", p=P)).then_inc(nw_loaded, 16)
            sp.dma_start(cnd, cond).then_inc(nw_loaded, 16)
            load_x(0, 0)
            load_stage(0, 0)
            load_stage(1, 1)
            sp.wait_ge(x_loaded, 16)
            load_x(1, 1)
            load_raw(0)
            for cc in range(1, NF // 4):
                for s in range(2):
                    c = 2 * cc + s
                    sp.wait_ge(wT_ready, 2 * c - 2)
                    load_stage(c, s)
                sp.wait_ge(raw_loaded, 16 * cc)
                load_raw(cc)

            sp.wait_ge(x_loaded, 32)
            sp.wait_ge(ternT_ready, NF)
            load_x(2, 2)
            sp.wait_ge(x_loaded, 48)
            load_x(3, 3)
            store_group(0, 0, 0)
            with sp.Fori(2, G - 2) as g:
                sp.wait_ge(x_loaded, 16 * g + 32)
                sp.wait_ge(stored, 16 * TG * g - 16 * TG)
                load_x(g + 2, (g + 2) % XSLOTS)
                store_group(g - 1, (g - 1) % XSLOTS, TG * g - TG)
            for g in (G - 3, G - 2, G - 1):
                store_group(g, g % XSLOTS, TG * g)
            sp.wait_ge(stored, 16 * NBATCH)

        @block.gpsimd
        def _(pool):
            pool.memset(ident[:, :], 0.0).then_inc(consts_zero, 1)
            pool.memset(ones[:, :], 1.0).then_inc(consts_zero, 1)
            for c, value in enumerate((1.0 / D, EPS, -0.5)):
                pool.memset(const_col(c), value).then_inc(consts_zero, 1)
            pool.wait_ge(consts_zero, 5)
            nc.gpsimd.affine_select(out=ident[:, :], in_=ident[:, :], compare_op=ALU.not_equal, fill=1.0,
                                    base=0, pattern=[[-1, P]], channel_multiplier=1).then_inc(consts_ready, 1)
            pool.wait_ge(consts_ready, 1)
            pool.tensor_copy(identb[:, :], ident[:, :]).then_inc(identb_ready, 1)

            def rms(m):
                pool.wait_ge(ssq_ready, m + 1)
                pool.tensor_tensor(msq[:, :], ssq[:, :], const_col(0), ALU.mult).then_inc(msq_ready, 1)
                pool.wait_ge(msq_ready, 2 * m + 1)
                pool.tensor_tensor(msq[:, :], msq[:, :], const_col(1), ALU.add).then_inc(msq_ready, 1)
                pool.wait_ge(msq_ready, 2 * m + 2)
                pool.tensor_tensor(rstd[:, :], msq[:, :], const_col(2), ALU.pow).then_inc(rstd_ready, 1)

            def scale_weights(j, pos):
                pool.wait_ge(winv_ready, j + 1)
                for half in range(2):
                    w = stage[:, pos // 2, half, pos % 2, :]
                    pool.tensor_tensor(w, w, winv[:, pos, half:half + 1].to_broadcast([P, D]),
                                       ALU.mult).then_inc(wscaled, 1)

            rms(0)
            pool.wait_ge(smax_ready, 1)
            pool.partition_all_reduce(smax_all[:, :], smax[:, :], P, ABSMAX).then_inc(smax_reduced, 1)
            scale_weights(0, 0)
            for i in range(1, TG):
                rms(i)
                if i < 3:
                    scale_weights(i, i)
            with pool.Fori(0, NI - 1) as i:
                rms(TG + i)
                for u in range(U):
                    scale_weights(i * U + u + 3, (u + 3) % 4)
            rms(2 * TG - 1)
            scale_weights(NF - 1, 3)
            with pool.Fori(2 * TG, NBATCH) as m:
                rms(m)

        @block.scalar
        def _(act):
            def square(m, slot, i, g):
                act.wait_ge(x_loaded, 16 * g + 16)
                if not isinstance(m, int) or m > 0:
                    act.wait_ge(xT_ready, m)
                act.activation(xn[:, :], x_tile(slot, i), ACT.Square, accum_out=ssq[:, :]).then_inc(ssq_ready, 1)

            def high_half(m, parity, i):
                act.wait_ge(hs_ready, m + 1)
                dst = hT[:, bass.ds(parity * 2 * HP, HP)].rearrange("p (k n) -> p k n", k=KD)
                act.copy(dst[:, :, bass.ds(i * P, P)], hs[:, :, :]).then_inc(hi_ready, 1)

            def gelu(n, j, b):
                act.wait_ge(gate_ready, n + 1)
                if not isinstance(n, int) or n > 1:
                    act.wait_ge(max_ready, n - 1)
                act.activation(glu[:, b, :], gate_ps[b], ACT.Gelu,
                               scale=unscale[:, bass.ds(j, 1), 1]).then_inc(gelu_ready, 1)

            def magnitude(n, j, b):
                act.wait_ge(h_ready, n + 1)
                act.activation(glu[:, b, :], tile_of(h, j), ACT.Abs).then_inc(abs_ready, 1)

            def weight_high(j):
                act.wait_ge(wT_ready, j + 1)
                for half in range(2):
                    dst = wT[:, bass.ds(j * WT + half * KD * 2 * P, KD * 2 * P)]
                    dst = dst.rearrange("p (k a n) -> p k a n", k=KD, a=2)[:, :, 0, :]
                    src = down_ps[half].rearrange("p (k n) -> p k n", k=KD)
                    act.copy(dst, src).then_inc(whi_ready, 1)

            for i in range(TG):
                square(i, 0, i, 0)
                if i < 2:
                    weight_high(i)
                high_half(i, 0, i)

            def phase0(i, last):
                n = i * U
                square(TG + i, 1, i, 1)
                gelu(n, n, 0)
                weight_high(n + 2)
                gelu(n + 1, n + 1, 1)
                magnitude(n, n, 0)
                weight_high(n + 3)
                gelu(n + 2, n + 2, 0)
                magnitude(n + 1, n + 1, 1)
                if not last:
                    weight_high(n + 4)
                high_half(TG + i, 1, i)
                gelu(n + 3, n + 3, 1)
                magnitude(n + 2, n + 2, 0)
                magnitude(n + 3, n + 3, 1)
                if not last:
                    weight_high(n + 5)

            phase0(0, False)
            with act.Fori(1, NI - 1) as i:
                phase0(i, False)
            phase0(NI - 1, True)
            act.wait_ge(wrecip_ready, 1)
            for t in range(KD):
                act.activation(raw(t), raw(t), ACT.Copy, scale=wrecip[:, :], bias=ROUND).then_inc(raw_magic, 1)

            def phase(g, prepare):
                with act.Fori(0, NI) as i:
                    n = g * NF + i * U
                    m = g * TG + TG + i
                    if prepare:
                        square(m, (g + 1) % XSLOTS, i, g + 1)
                    gelu(n, i * U, 0)
                    gelu(n + 1, i * U + 1, 1)
                    magnitude(n, i * U, 0)
                    gelu(n + 2, i * U + 2, 0)
                    magnitude(n + 1, i * U + 1, 1)
                    if prepare:
                        high_half(m, (g + 1) % 2, i)
                    gelu(n + 3, i * U + 3, 1)
                    magnitude(n + 2, i * U + 2, 0)
                    magnitude(n + 3, i * U + 3, 1)

            with act.Fori(1, G - 1) as g:
                phase(g, True)
            phase(G - 1, False)

        @block.vector
        def _(dve):
            def row_scales(j, quad, pos):
                dve.wait_ge(stage_loaded[pos // 2], 32 * quad + 32)
                dve.tensor_reduce(wmax[:, :], stage[:, pos // 2, :, pos % 2, :], AX_X, ALU.max,
                                  apply_absolute_value=True).then_inc(wmax_ready, 1)
                dve.wait_ge(wmax_ready, j + 1)
                dve.tensor_scalar(wmax[:, :], wmax[:, :], TINY, None, ALU.max).then_inc(wclamped, 1)
                dve.wait_ge(wclamped, j + 1)
                dve.tensor_scalar(wpow[:, :].bitcast(I32), wmax[:, :].bitcast(I32), EXPONENT, None,
                                  ALU.bitwise_and).then_inc(wpow_ready, 1)
                dve.wait_ge(wpow_ready, j + 1)
                dve.tensor_scalar(winv[:, pos, :].bitcast(I32), wpow[:, :].bitcast(I32), EXPONENT, None,
                                  ALU.bitwise_xor).then_inc(wcomplement, 1)
                dve.wait_ge(wcomplement, j + 1)
                dve.tensor_scalar(winv[:, pos, :], winv[:, pos, :], W_UP, None, ALU.mult).then_inc(winv_ready, 1)
                dve.tensor_scalar(unscale[:, bass.ds(j, 1), :].rearrange("p o h -> p (o h)"), wpow[:, :],
                                  sundo[:, :], UNDO_W, ALU.mult, ALU.mult).then_inc(unscale_ready, 1)

            def weight_low(j):
                dve.wait_ge(whi_ready, 2 * j + 2)
                for half in range(2):
                    dst = wT[:, bass.ds(j * WT + half * KD * 2 * P, KD * 2 * P)]
                    dst = dst.rearrange("p (k a n) -> p k a n", k=KD, a=2)
                    src = down_ps[half].rearrange("p (k n) -> p k n", k=KD)
                    dve.tensor_tensor(dst[:, :, 1, :], src, dst[:, :, 0, :], ALU.subtract).then_inc(wlo_ready, 1)

            def normalise(m, slot, i):
                dve.wait_ge(rstd_ready, m + 1)
                dve.tensor_scalar(xn[:, :], x_tile(slot, i), rstd[:, :], None, ALU.mult).then_inc(xn_ready, 1)

            def scale_tile(m):
                dve.wait_ge(xT_ready, m + 1)
                s = scaleT[:, bass.ds(m, 1), :].rearrange("p o k -> p (o k)").unsqueeze(2).to_broadcast([P, KD, P])
                dve.tensor_tensor(hs[:, :, :], xT_ps.rearrange("p (k n) -> p k n", k=KD), s,
                                  ALU.mult).then_inc(hs_ready, 1)

            def low_half(m, parity, i):
                dve.wait_ge(hi_ready, m + 1)
                def half(part):
                    v = hT[:, bass.ds(parity * 2 * HP + part * HP, HP)].rearrange("p (k n) -> p k n", k=KD)
                    return v[:, :, bass.ds(i * P, P)]
                dve.tensor_tensor(half(1), hs[:, :, :], half(0), ALU.subtract).then_inc(lo_ready, 1)

            def glu_tile(n, j, b, reused=True):
                if reused:
                    dve.wait_ge(q_ready, n - NF + 1)
                dve.wait_ge(gelu_ready, n + 1)
                dve.wait_ge(val_ready, n + 1)
                dve.scalar_tensor_tensor(out=tile_of(h, j), in0=val_ps[b], scalar=unscale[:, bass.ds(j, 1), 0],
                                         in1=glu[:, b, :], op0=ALU.mult, op1=ALU.mult).then_inc(h_ready, 1)

            def max_tile(n, b, g):
                dve.wait_ge(abs_ready, n + 1)
                if not isinstance(n, int) or n > 0:
                    dve.wait_ge(max_ready, n)
                dve.wait_ge(runmax_zero, g + 1)
                dve.tensor_tensor(runmax[:, :], glu[:, b, :], runmax[:, :], ALU.max).then_inc(max_ready, 1)

            def quant_scale(n, j, g):
                dve.wait_ge(sbc_ready, TG * g + TG)
                dve.tensor_tensor(tile_of(h, j), tile_of(h, j), stat_ps, ALU.mult).then_inc(hscaled, 1)

            def quant_round(n, j):
                dve.wait_ge(hscaled, n + 1)
                dve.tensor_scalar(tile_of(q, j), tile_of(h, j), ROUND, ROUND, ALU.add,
                                  ALU.subtract).then_inc(q_ready, 1)

            def token_scales(g):
                dve.wait_ge(maxT_ready, TG * g + TG)
                dve.tensor_reduce(mtok[:, :], stat_ps.rearrange("p (i f) -> p i f", i=TG), AX_X,
                                  ALU.max).then_inc(mraw_ready, 1)
                dve.memset(runmax[:, :], 0.0).then_inc(runmax_zero, 1)
                dve.wait_ge(mraw_ready, g + 1)
                dve.tensor_scalar(mtok[:, :], mtok[:, :], CLIP, None, ALU.max).then_inc(mtok_ready, 1)
                dve.wait_ge(mtok_ready, g + 1)
                dve.reciprocal(minv[:, :], mtok[:, :]).then_inc(minv_ready, 1)
                dve.wait_ge(minv_ready, g + 1)
                dve.tensor_scalar(stok[:, :], minv[:, :], QMAX, None, ALU.mult).then_inc(stok_ready, 1)

            def output_scales(g):
                if not isinstance(g, int) or g > 0:
                    dve.wait_ge(y_ready, TG * g)
                dve.tensor_scalar(ctok[:, :], mtok[:, :], wmean127[:, :], None, ALU.mult).then_inc(ctok_ready, 1)

            def add_residual(m, ps, slot, i, g):
                dve.wait_ge(down_ready, m + 1)
                dve.wait_ge(ctok_ready, g + 1)
                xt = x_tile(slot, i)
                dve.scalar_tensor_tensor(out=xt, in0=ps, scalar=ctok[:, i:i + 1], in1=xt, op0=ALU.mult,
                                         op1=ALU.add).then_inc(y_ready, 1)

            dve.memset(runmax[:, :], 0.0).then_inc(runmax_zero, 1)

            dve.wait_ge(nwT_ready, KD + 1)
            dve.tensor_copy(nwT, xT_ps).then_inc(nwT_copied, 1)
            dve.tensor_copy(cndT, stat_ps[:, 0:NBATCH]).then_inc(nwT_copied, 1)
            dve.wait_ge(scale_mm, KD)
            dve.tensor_scalar(scaleT[:, :, :].rearrange("p b k -> p k b"),
                              down_ps[0][:, 0:KD * NBATCH].rearrange("p (k b) -> p k b", k=KD), 1.0, None,
                              ALU.add).then_inc(scale_one, 1)
            dve.wait_ge(scale_one, 1)
            flat = scaleT[:, :, :].rearrange("p b k -> p (b k)")
            dve.tensor_reduce(smax[:, :], flat, AX_X, ALU.max, apply_absolute_value=True).then_inc(smax_ready, 1)
            dve.wait_ge(smax_reduced, 1)
            dve.tensor_scalar(smax[:, :], smax_all[:, :], TINY, None, ALU.max).then_inc(spow_ready, 1)
            dve.wait_ge(spow_ready, 1)
            dve.tensor_scalar(spow[:, :].bitcast(I32), smax[:, :].bitcast(I32), EXPONENT, None,
                              ALU.bitwise_and).then_inc(spow_ready, 1)
            dve.wait_ge(spow_ready, 2)
            dve.tensor_scalar(sinv[:, :].bitcast(I32), spow[:, :].bitcast(I32), EXPONENT, None,
                              ALU.bitwise_xor).then_inc(spow_ready, 1)
            dve.tensor_scalar(sundo[:, :], spow[:, :], UNDO_H, None, ALU.mult).then_inc(spow_ready, 1)
            dve.wait_ge(spow_ready, 4)
            dve.tensor_scalar(flat, flat, sinv[:, :], H_UP, ALU.mult, ALU.mult).then_inc(scale_ready, 1)
            row_scales(0, 0, 0)
            normalise(0, 0, 0)
            dve.wait_ge(scale_ready, 1)
            row_scales(1, 0, 1)
            scale_tile(0)
            weight_low(0)
            low_half(0, 0, 0)
            row_scales(2, 0, 2)
            normalise(1, 0, 1)
            scale_tile(1)
            weight_low(1)
            low_half(1, 0, 1)
            for i in range(2, TG):
                normalise(i, 0, i)
                scale_tile(i)
                low_half(i, 0, i)

            def weight_sum(t):
                dve.wait_ge(raw_loaded, 16 * t + 16)
                dve.tensor_reduce(asum[:, bass.ds(t, 1)], raw(t), AX_X, ALU.add,
                                  apply_absolute_value=True).then_inc(asum_ready, 1)

            def weight_mean():
                dve.wait_ge(wsum_ready, 1)
                dve.tensor_scalar(wmean[:, :], stat_ps[:, 0:1], 1.0 / (D * FF), CLIP, ALU.mult,
                                  ALU.max).then_inc(wmean_ready, 1)
                dve.wait_ge(wmean_ready, 1)
                dve.reciprocal(wrecip[:, :], wmean[:, :]).then_inc(wrecip_ready, 1)
                dve.tensor_scalar(wmean127[:, :], wmean[:, :], 1.0 / QMAX, None, ALU.mult).then_inc(wmean_ready, 1)

            def phase0(i, last):
                n = i * U
                for u in range(U):
                    glu_tile(n + u, n + u, u % 2, False)
                    if u > 0:
                        max_tile(n + u - 1, (u - 1) % 2, 0)
                    if not last or u == 0:
                        row_scales(n + u + 3, i if u == 0 else i + 1, (u + 3) % 4)
                    if u == 0:
                        normalise(TG + i, 1, i)
                    if u == 1:
                        scale_tile(TG + i)
                    if u == 3:
                        max_tile(n + u, u % 2, 0)
                    if not last or u < 2:
                        weight_low(n + u + 2)
                    if u == 2:
                        low_half(TG + i, 1, i)
                    if not last and u == 3:
                        weight_sum(i)
                    if last and u == 0:
                        weight_sum(i)
                        dve.wait_ge(asum_ready, KD)
                        dve.tensor_reduce(asum1[:, :], asum[:, :], AX_X, ALU.add).then_inc(asum1_ready, 1)
                    if last and u == 2:
                        weight_mean()

            phase0(0, False)
            with dve.Fori(1, NI - 1) as i:
                phase0(i, False)
            phase0(NI - 1, True)

            token_scales(0)
            for t in range(KD):
                dve.wait_ge(raw_magic, t + 1)
                dve.tensor_scalar(vb[:, t, :], raw(t), ROUND, 1.0, ALU.subtract, ALU.min).then_inc(vb_ready, 1)
            for k in range(NF):
                dve.wait_ge(ternT_ready, k + 1)
                dve.tensor_scalar(tern[:, k * D:(k + 1) * D], down_ps[k % 2].bitcast(BF16)[:, 0:D], -1.0, None,
                                  ALU.max).then_inc(tern_ready, 1)
            dve.wait_ge(wmean_ready, 2)
            output_scales(0)

            def phase(g, prepare):
                with dve.Fori(0, NI) as i:
                    n = g * NF + i * U
                    m = g * TG + TG + i
                    for u in range(U):
                        j = i * U + u
                        quant_scale(n + u - NF, j, g - 1)
                        quant_round(n + u - NF, j)
                        glu_tile(n + u, j, u % 2)
                        if u > 0:
                            max_tile(n + u - 1, (u - 1) % 2, g)
                        if prepare and u == 0:
                            normalise(m, (g + 1) % XSLOTS, i)
                        if prepare and u == 1:
                            scale_tile(m)
                        if prepare and u == 2:
                            low_half(m, (g + 1) % 2, i)
                    max_tile(n + U - 1, 1, g)
                for i in range(TG):
                    if i == 2:
                        token_scales(g)
                    add_residual(g * TG - TG + i, down_ps[i % 2], (g - 1) % XSLOTS, i, g - 1)
                output_scales(g)

            with dve.Fori(1, G - 1) as g:
                phase(g, True)
            phase(G - 1, False)

            with dve.Fori(0, NF) as j:
                quant_scale(j + NF * (G - 1), j, G - 1)
                quant_round(j + NF * (G - 1), j)
            for i in range(TG):
                add_residual(TG * (G - 1) + i, last_ps[i], (G - 1) % XSLOTS, i, G - 1)

        @block.tensor
        def _(pe):
            def turn(dst, src, ident_ap):
                return pe.transpose(dst, src, ident_ap)

            def turn_x(m):
                pe.wait_ge(xn_ready, m + 1)
                if not isinstance(m, int) or m > 0:
                    pe.wait_ge(hs_ready, m)
                for k in range(KD):
                    last = turn(xT_ps[:, k * P:(k + 1) * P], xn[:, k * P:(k + 1) * P], ident[:, :])
                last.then_inc(xT_ready, 1)

            def turn_weights(j, pos):
                pe.wait_ge(wscaled, 2 * j + 2)
                if not isinstance(j, int) or j > 0:
                    pe.wait_ge(wlo_ready, 2 * j)
                for half in range(2):
                    for k in range(KD):
                        last = turn(down_ps[half][:, k * P:(k + 1) * P],
                                    stage[:, pos // 2, half, pos % 2, k * P:(k + 1) * P], ident[:, :])
                last.then_inc(wT_ready, 1)

            def up_half(j, half, ps, parity):
                n_mm = 3 * KD
                c = 0
                for k in range(KD):
                    for w_part, h_part in ((0, 0), (0, 1), (1, 0)):
                        rhs = hT[:, bass.ds(parity * 2 * HP + h_part * HP + k * NT, NT)]
                        last = pe.matmul(ps, weight(j, half, k, w_part), rhs, start=(c == 0), stop=(c == n_mm - 1))
                        c += 1
                return last

            def up_tile(n, j, b, parity):
                if not isinstance(n, int) or n > 1:
                    pe.wait_ge(gelu_ready, n - 1)
                up_half(j, 1, gate_ps[b], parity).then_inc(gate_ready, 1)
                if not isinstance(n, int) or n > 1:
                    pe.wait_ge(h_ready, n - 1)
                up_half(j, 0, val_ps[b], parity).then_inc(val_ready, 1)

            def turn_max(g):
                pe.wait_ge(max_ready, NF * g + NF)
                for i in range(TG):
                    turn(stat_ps[:, i * P:(i + 1) * P], runmax[:, i * P:(i + 1) * P],
                         ident[:, :]).then_inc(maxT_ready, 1)

            def spread_scales(g):
                pe.wait_ge(stok_ready, g + 1)
                for i in range(TG):
                    turn(stat_ps[:, i * P:(i + 1) * P], stok[:, i:i + 1].to_broadcast([P, P]),
                         ident[:, :]).then_inc(sbc_ready, 1)

            def down_mm(ps, k, i):
                return pe.matmul(ps, q[:, bass.ds(k * NT + i * P, P)], tern[:, bass.ds(k * D, D)],
                                 start=(isinstance(k, int) and k == 0), stop=(isinstance(k, int) and k == NF - 1))

            pe.wait_ge(consts_ready, 1)
            pe.wait_ge(nw_loaded, 32)
            for k in range(KD):
                turn(xT_ps[:, k * P:(k + 1) * P], nw[:, k, :], ident[:, :]).then_inc(nwT_ready, 1)
            turn(stat_ps[:, 0:NBATCH], cnd, ident[0:NBATCH, 0:NBATCH]).then_inc(nwT_ready, 1)
            pe.wait_ge(nwT_copied, 2)
            for k in range(KD):
                pe.matmul(down_ps[0][:, k * NBATCH:(k + 1) * NBATCH], nwT[:, k * P:(k + 1) * P], cndT,
                          start=True, stop=True).then_inc(scale_mm, 1)
            turn_x(0)
            pe.wait_ge(scale_one, 1)
            turn_weights(0, 0)
            turn_x(1)
            turn_weights(1, 1)
            turn_x(2)
            turn_x(3)

            def phase0(i, last):
                n = i * U
                for u in range(U):
                    pe.wait_ge(wlo_ready, 2 * (n + u) + 2)
                    up_tile(n + u, n + u, u % 2, 0)
                    if not last or u < 2:
                        turn_weights(n + u + 2, (u + 2) % 4)
                    if u == 0:
                        turn_x(TG + i)
                    if last and u == 1:
                        pe.wait_ge(asum1_ready, 1)
                        pe.matmul(stat_ps[:, 0:1], ones[:, :], asum1[:, :], start=True,
                                  stop=True).then_inc(wsum_ready, 1)

            pe.wait_ge(lo_ready, TG)
            phase0(0, False)
            with pe.Fori(1, NI - 1) as i:
                phase0(i, False)
            phase0(NI - 1, True)

            pe.wait_ge(wmean_ready, 1)
            turn_max(0)
            pe.wait_ge(identb_ready, 1)
            pe.wait_ge(vb_ready, KD)
            for k in range(NF):
                if k == 0:
                    pe.wait_ge(wlo_ready, 2 * NF)
                if k >= 2:
                    pe.wait_ge(tern_ready, k - 1)
                for t in range(KD):
                    last = turn(down_ps[k % 2].bitcast(BF16)[:, t * P:(t + 1) * P], vb[:, t, k * P:(k + 1) * P],
                                identb[:, :])
                last.then_inc(ternT_ready, 1)
            spread_scales(0)

            def phase(g, prepare):
                with pe.Fori(0, NI) as i:
                    n = g * NF + i * U
                    pe.wait_ge(lo_ready, TG * g + TG)
                    for u in range(U):
                        up_tile(n + u, i * U + u, u % 2, g % 2)
                        if prepare and u == 0:
                            turn_x(g * TG + TG + i)
                pe.wait_ge(q_ready, NF * g)
                pe.wait_ge(tern_ready, NF)
                for i in range(TG):
                    if i >= 2:
                        pe.wait_ge(y_ready, TG * g - TG + i - 1)
                    for k in range(NF):
                        last = down_mm(down_ps[i % 2], k, i)
                    last.then_inc(down_ready, 1)
                    if i == 0:
                        turn_max(g)
                    if i == 2:
                        spread_scales(g)

            with pe.Fori(1, G - 1) as g:
                phase(g, True)
            phase(G - 1, False)

            for k in range(NF):
                pe.wait_ge(q_ready, NF * (G - 1) + k + 1)
                for i in range(TG):
                    last = down_mm(last_ps[i], k, i)
                    if k == NF - 1:
                        last.then_inc(down_ready, 1)


_INS = ["x", "cond_256", "L0_cond_norm_w", "L0_cond_up_w", "L0_cond_down_w"]
_OUTS = [((64, 128, 512), "float32")]


def kernel(**inputs):
    import numpy as _np
    import concourse.bacc as _bacc
    from concourse import mybir as _mybir
    from concourse.bass_utils import run_bass_kernel_spmd as _run

    nc = _bacc.Bacc("TRN2", target_bir_lowering=False, num_devices=1)
    arrays, args = {}, []
    for name in _INS:
        a = _np.ascontiguousarray(inputs[name])
        arrays[f"in_{name}_dram"] = a
        args.append(nc.dram_tensor(f"in_{name}_dram", a.shape, _mybir.dt.from_np(a.dtype), kind="ExternalInput").ap())
    for i, (shape, dtype) in enumerate(_OUTS):
        dt = _mybir.dt.from_np(_np.dtype(dtype))
        args.append(nc.dram_tensor(f"out_{i}_dram", shape, dt, kind="ExternalOutput").ap())
    bass_bitlinear_glu_kernel(nc, *args)
    r = _run(nc, [arrays], core_ids=[0])
    got = tuple(r.results[0][f"out_{i}_dram"] for i in range(len(_OUTS)))
    return got[0]
```

```python
from contextlib import ExitStack

import concourse.bass as bass
from concourse import mybir

F32 = mybir.dt.float32
F16 = mybir.dt.float16
BF16 = mybir.dt.bfloat16
I32 = mybir.dt.int32
ALU = mybir.AluOpType
ACT = mybir.ActivationFunctionType
AX_X = mybir.AxisListType.X
ABSMAX = bass.bass_isa.ReduceOp.absmax

P = 128
EPS = 1e-6
CLIP = 1e-5
QMAX = 127.0
ROUND = 12582912.0
EXPONENT = 0x7F800000
W_UP = 2.0 ** 12
H_UP = 2.0 ** 9
UNDO_W = 2.0 ** -13
UNDO_H = 2.0 ** -10
TINY = 1e-30


def bass_bitlinear_glu_kernel(
    nc: bass.Bass,
    x: bass.AP,
    cond: bass.AP,
    norm_w: bass.AP,
    up_w: bass.AP,
    down_w: bass.AP,
    out: bass.AP,
):
    NBATCH, T, D = x.shape
    C = cond.shape[1]
    FF = down_w.shape[1]
    KD = D // P
    NF = FF // P
    TG = 4
    NT = TG * P
    G = NBATCH // TG
    U = 4
    NI = NF // U
    assert T == P and C == P and NI == TG and NT == 512 and D == 512
    WT = 2 * KD * 2 * P
    XG = TG * D
    HP = KD * NT
    XSLOTS = 4

    x_g = x.rearrange("(g b) t d -> g t b d", b=TG)
    out_b = out
    upw_c = up_w.rearrange("(h c j p) d -> h c p j d", h=2, j=2, p=P)
    downw_t = down_w.rearrange("(t p) f -> t p f", p=P)

    with ExitStack() as ctx:
        def sb(name, shape, dt):
            return ctx.enter_context(nc.sbuf_tensor(name, shape, dt))

        def sem(name):
            return ctx.enter_context(nc.semaphore(name))

        wT = sb("wT", [P, NF * WT], F16)
        tern_q = sb("tern_q", [P, NF * (D + NT)], BF16)
        tern = tern_q[:, 0:NF * D]
        q = tern_q[:, NF * D:]
        h = sb("h", [P, NF * NT], F32)
        xbuf = sb("xbuf", [P, XSLOTS * XG], F32)
        hT = sb("hT", [P, 2 * 2 * HP], F16)
        vb = sb("vb", [P, KD, FF], BF16)
        xn = sb("xn", [P, D], F32)
        hs = sb("hs", [P, KD, P], F32)
        glu = sb("glu", [P, 2, NT], F32)
        runmax = sb("runmax", [P, NT], F32)
        scaleT = sb("scaleT", [P, NBATCH, KD], F32)
        ident = sb("ident", [P, P], F32)
        identb = sb("identb", [P, P], BF16)
        ones = sb("ones", [P, P], F32)
        unscale = sb("unscale", [P, NF, 2], F32)
        wmax = sb("wmax", [P, 4], F32)
        wpow = sb("wpow", [P, 4], F32)
        winv = sb("winv", [P, 2, 4], F32)
        ssq = sb("ssq", [P, 1], F32)
        msq = sb("msq", [P, 1], F32)
        rstd = sb("rstd", [P, 1], F32)
        first_rms = sb("first_rms", [P, 2 * TG], F32)
        rms_consts = sb("rms_consts", [P, 3, TG], F32)
        smax = sb("smax", [P, 1], F32)
        smax_all = sb("smax_all", [P, 1], F32)
        spow = sb("spow", [P, 1], F32)
        sinv = sb("sinv", [P, 1], F32)
        sundo = sb("sundo", [P, 1], F32)
        mtok = sb("mtok", [P, TG], F32)
        minv = sb("minv", [P, TG], F32)
        stok = sb("stok", [P, TG], F32)
        ctok = sb("ctok", [P, TG], F32)
        asum = sb("asum", [P, KD], F32)
        asum1 = sb("asum1", [P, 1], F32)
        wmean = sb("wmean", [P, 1], F32)
        wrecip = sb("wrecip", [P, 1], F32)
        wmean127 = sb("wmean127", [P, 1], F32)

        banks = ctx.enter_context(nc.psum_tensor("banks", [P, 8, 512], F32))
        gate_ps = [banks[:, 0, :], banks[:, 1, :]]
        val_ps = [banks[:, 2, :], banks[:, 3, :]]
        last_ps = gate_ps + val_ps
        down_ps = [banks[:, 4, :], banks[:, 5, :]]
        xT_ps = banks[:, 6, :]
        stat_ps = banks[:, 7, :]

        stage = xbuf[:, 2 * XG:4 * XG].rearrange("p (s j h d) -> p s j h d", s=2, j=2, h=2)
        raw_flat = tern_q[:, :].bitcast(F32)
        ssq4, rstd4 = first_rms[:, 0:TG], first_rms[:, TG:2 * TG]
        xn4 = h[:, 4 * NT:8 * NT].rearrange("p (i d) -> p i d", i=TG)
        hs4 = h[:, 8 * NT:12 * NT].rearrange("p (i d) -> p i d", i=TG)
        unused_abs = h[:, 12 * NT:16 * NT]
        nw = h[:, 0:KD * P].rearrange("p (k c) -> p k c", k=KD)
        cnd = h[0:NBATCH, 512:512 + P]
        nwT = h[:, 1024:1024 + D]
        cndT = h[:, 1536:1536 + NBATCH]

        x_loaded = sem("x_loaded")
        nw_loaded = sem("nw_loaded")
        stage_loaded = [sem("stage_loaded0"), sem("stage_loaded1")]
        raw_loaded = sem("raw_loaded")
        consts_zero = sem("consts_zero")
        consts_ready = sem("consts_ready")
        identb_ready = sem("identb_ready")
        nwT_ready = sem("nwT_ready")
        nwT_copied = sem("nwT_copied")
        scale_mm = sem("scale_mm")
        scale_one = sem("scale_one")
        smax_ready = sem("smax_ready")
        smax_reduced = sem("smax_reduced")
        spow_ready = sem("spow_ready")
        scale_ready = sem("scale_ready")
        ssq_ready = sem("ssq_ready")
        msq_ready = sem("msq_ready")
        rstd_ready = sem("rstd_ready")
        xn_ready = sem("xn_ready")
        xT_ready = sem("xT_ready")
        hs_ready = sem("hs_ready")
        hi_ready = sem("hi_ready")
        lo_ready = sem("lo_ready")
        wmax_ready = sem("wmax_ready")
        wclamped = sem("wclamped")
        wpow_ready = sem("wpow_ready")
        wcomplement = sem("wcomplement")
        winv_ready = sem("winv_ready")
        unscale_ready = sem("unscale_ready")
        wscaled = sem("wscaled")
        first_scaled = sem("first_scaled")
        wT_ready = sem("wT_ready")
        whi_ready = sem("whi_ready")
        wlo_ready = sem("wlo_ready")
        asum_ready = sem("asum_ready")
        asum1_ready = sem("asum1_ready")
        wsum_ready = sem("wsum_ready")
        wmean_ready = sem("wmean_ready")
        wrecip_ready = sem("wrecip_ready")
        raw_magic = sem("raw_magic")
        vb_ready = sem("vb_ready")
        ternT_ready = sem("ternT_ready")
        tern_ready = sem("tern_ready")
        gate_ready = sem("gate_ready")
        val_ready = sem("val_ready")
        gelu_ready = sem("gelu_ready")
        h_ready = sem("h_ready")
        abs_ready = sem("abs_ready")
        runmax_zero = sem("runmax_zero")
        max_ready = sem("max_ready")
        maxT_ready = sem("maxT_ready")
        mraw_ready = sem("mraw_ready")
        mtok_ready = sem("mtok_ready")
        minv_ready = sem("minv_ready")
        stok_ready = sem("stok_ready")
        ctok_ready = sem("ctok_ready")
        sbc_ready = sem("sbc_ready")
        hscaled = sem("hscaled")
        q_ready = sem("q_ready")
        hround = sem("hround")
        q_odd_ready = sem("q_odd_ready")
        down_ready = sem("down_ready")
        y_ready = sem("y_ready")
        stored = sem("stored")

        def weight(j, half, k, part):
            return wT[:, bass.ds(j * WT + ((half * KD + k) * 2 + part) * P, P)]

        def const_col(c):
            return rms_consts[:, c, 0:1]

        def x_tile(slot, i):
            return xbuf[:, bass.ds(slot * XG + i * D, D)]

        def raw(t):
            return raw_flat[:, bass.ds(t * FF, FF)]

        def tile_of(buf, j):
            return buf[:, bass.ds(j * NT, NT)]

        block = ctx.enter_context(nc.Block())

        @block.sync
        def _(sp):
            def load_x(g, slot):
                sp.dma_start(xbuf[:, bass.ds(slot * XG, XG)].rearrange("p (b d) -> p b d", b=TG),
                             x_g[g]).then_inc(x_loaded, 16)

            def load_stage(c, s):
                for half in range(2):
                    sp.dma_start(stage[:, s, :, half, :], upw_c[half, c]).then_inc(stage_loaded[s], 16)

            def load_raw(t):
                sp.dma_start(raw(t), downw_t[t]).then_inc(raw_loaded, 16)

            def store_group(g, slot, first):
                for i in range(TG):
                    sp.wait_ge(y_ready, first + i + 1)
                    sp.dma_start(out_b[g * TG + i], x_tile(slot, i)).then_inc(stored, 16)

            sp.dma_start(nw, norm_w.rearrange("(k p) c -> p k c", p=P)).then_inc(nw_loaded, 16)
            sp.dma_start(cnd, cond).then_inc(nw_loaded, 16)
            load_x(0, 0)
            load_stage(0, 0)
            load_stage(1, 1)
            sp.wait_ge(x_loaded, 16)
            load_x(1, 1)
            for t in range(KD):
                load_raw(t)
            for cc in range(1, NF // 4):
                for s in range(2):
                    c = 2 * cc + s
                    sp.wait_ge(wT_ready, 2 * c - 2)
                    load_stage(c, s)

            sp.wait_ge(x_loaded, 32)
            sp.wait_ge(wT_ready, NF)
            load_x(2, 2)
            sp.wait_ge(x_loaded, 48)
            load_x(3, 3)
            store_group(0, 0, 0)
            with sp.Fori(2, G - 2) as g:
                sp.wait_ge(x_loaded, 16 * g + 32)
                sp.wait_ge(stored, 16 * TG * g - 16 * TG)
                load_x(g + 2, (g + 2) % XSLOTS)
                store_group(g - 1, (g - 1) % XSLOTS, TG * g - TG)
            for g in (G - 3, G - 2, G - 1):
                store_group(g, g % XSLOTS, TG * g)
            sp.wait_ge(stored, 16 * NBATCH)

        @block.gpsimd
        def _(pool):
            pool.memset(ident[:, :], 0.0).then_inc(consts_zero, 1)
            pool.memset(ones[:, :], 1.0).then_inc(consts_zero, 1)
            for c, value in enumerate((1.0 / D, EPS, -0.5)):
                pool.memset(rms_consts[:, c, :], value).then_inc(consts_zero, 1)
            pool.wait_ge(consts_zero, 5)
            nc.gpsimd.affine_select(out=ident[:, :], in_=ident[:, :], compare_op=ALU.not_equal, fill=1.0,
                                    base=0, pattern=[[-1, P]], channel_multiplier=1).then_inc(consts_ready, 1)
            pool.wait_ge(consts_ready, 1)
            pool.tensor_copy(identb[:, :], ident[:, :]).then_inc(identb_ready, 1)

            def rms(m):
                pool.wait_ge(ssq_ready, m + 1)
                pool.tensor_tensor(msq[:, :], ssq[:, :], const_col(0), ALU.mult).then_inc(msq_ready, 1)
                pool.wait_ge(msq_ready, 2 * m + 1)
                pool.tensor_tensor(msq[:, :], msq[:, :], const_col(1), ALU.add).then_inc(msq_ready, 1)
                pool.wait_ge(msq_ready, 2 * m + 2)
                pool.tensor_tensor(rstd[:, :], msq[:, :], const_col(2), ALU.pow).then_inc(rstd_ready, 1)

            def scale_weights(c, slot):
                pool.wait_ge(winv_ready, c + 1)
                for j in range(2):
                    for half in range(2):
                        w = stage[:, slot, j, half, :]
                        inv = winv[:, slot, 2 * j + half:2 * j + half + 1].to_broadcast([P, D])
                        pool.tensor_tensor(w, w, inv, ALU.mult).then_inc(wscaled, 1)

            pool.wait_ge(smax_ready, 1)
            pool.partition_all_reduce(smax_all[:, :], smax[:, :], P, ABSMAX).then_inc(smax_reduced, 1)
            pool.wait_ge(ssq_ready, TG)
            pool.tensor_tensor(ssq4, ssq4, rms_consts[:, 0, :], ALU.mult).then_inc(msq_ready, TG)
            pool.wait_ge(msq_ready, TG)
            pool.tensor_tensor(ssq4, ssq4, rms_consts[:, 1, :], ALU.add).then_inc(msq_ready, TG)
            pool.wait_ge(msq_ready, 2 * TG)
            pool.tensor_tensor(rstd4, ssq4, rms_consts[:, 2, :], ALU.pow).then_inc(rstd_ready, TG)
            pool.wait_ge(winv_ready, 1)
            for half in range(2):
                w = stage[:, 0, 1, half, :]
                inv = winv[:, 0, 2 + half:3 + half].to_broadcast([P, D])
                pool.tensor_tensor(w, w, inv, ALU.mult).then_inc(wscaled, 2)
            scale_weights(1, 1)
            with pool.Fori(0, NI - 1) as i:
                rms(TG + i)
                for slot in range(2):
                    scale_weights(2 * i + 2 + slot, slot)
            with pool.Fori(2 * TG - 1, NBATCH) as m:
                rms(m)

        @block.scalar
        def _(act):
            def square(m, slot, i, g):
                act.wait_ge(x_loaded, 16 * g + 16)
                if not isinstance(m, int) or m > 0:
                    act.wait_ge(xT_ready, m)
                act.activation(xn[:, :], x_tile(slot, i), ACT.Square, accum_out=ssq[:, :]).then_inc(ssq_ready, 1)

            def high_half(m, parity, i, src=hs):
                act.wait_ge(hs_ready, m + 1)
                dst = hT[:, bass.ds(parity * 2 * HP, HP)].rearrange("p (k n) -> p k n", k=KD)
                act.copy(dst[:, :, bass.ds(i * P, P)], src[:, :, :]).then_inc(hi_ready, 1)

            def gelu(n, j, b):
                act.wait_ge(gate_ready, n + 1)
                if not isinstance(n, int) or n > 1:
                    act.wait_ge(max_ready, n - 1)
                act.activation(glu[:, b, :], gate_ps[b], ACT.Gelu,
                               scale=unscale[:, bass.ds(j, 1), 1]).then_inc(gelu_ready, 1)

            def magnitude(n, j, b):
                act.wait_ge(h_ready, n + 1)
                act.activation(glu[:, b, :], tile_of(h, j), ACT.Abs).then_inc(abs_ready, 1)

            def weight_high(j, ps=down_ps):
                act.wait_ge(wT_ready, j + 1)
                for half in range(2):
                    dst = wT[:, bass.ds(j * WT + half * KD * 2 * P, KD * 2 * P)]
                    dst = dst.rearrange("p (k a n) -> p k a n", k=KD, a=2)[:, :, 0, :]
                    src = ps[half].rearrange("p (k n) -> p k n", k=KD)
                    act.copy(dst, src).then_inc(whi_ready, 1)

            act.wait_ge(x_loaded, 16)
            for i in range(TG):
                act.activation(hs4[:, i, :], x_tile(0, i), ACT.Square, accum_out=ssq4[:, i:i + 1]).then_inc(ssq_ready, 1)
            act.wait_ge(rstd_ready, TG)
            for i in range(TG):
                act.activation(xn4[:, i, :], x_tile(0, i), ACT.Copy, scale=rstd4[:, i:i + 1]).then_inc(xn_ready, 1)
            act.wait_ge(winv_ready, 1)
            for half in range(2):
                w = stage[:, 0, 0, half, :]
                act.activation(w, w, ACT.Copy, scale=winv[:, 0, half:half + 1]).then_inc(first_scaled, 1)
            for i in range(TG):
                high_half(i, 0, i, hs4[:, i, :].rearrange("p (k n) -> p k n", k=KD))
            weight_high(0)
            weight_high(1, [xT_ps, stat_ps])

            def sum_magnitudes(t):
                act.wait_ge(raw_loaded, 16 * KD)
                if t:
                    act.wait_ge(asum_ready, t)
                act.activation(unused_abs, raw(t), ACT.Abs, accum_out=asum[:, bass.ds(t, 1)]).then_inc(asum_ready, 1)

            def add_round(t):
                act.wait_ge(wrecip_ready, 1)
                act.activation(raw(t), raw(t), ACT.Copy, scale=wrecip[:, :], bias=ROUND).then_inc(raw_magic, 1)

            def phase0(i, first, last):
                n = i * U
                for u in range(U):
                    b = u % 2
                    if u == 0:
                        square(TG + i, 1, i, 1)
                    gelu(n + u, n + u, b)
                    if u > 0:
                        magnitude(n + u - 1, n + u - 1, 1 - b)
                    if u == 3:
                        high_half(TG + i, 1, i)
                        magnitude(n + 3, n + 3, 1)
                    if not last or u < 2:
                        weight_high(n + u + 2)
                    if first and u < 2:
                        sum_magnitudes(2 * u)
                        sum_magnitudes(2 * u + 1)
                    if not first and not last and u < 2:
                        add_round(2 * i - 2 + u)

            phase0(0, True, False)
            with act.Fori(1, NI - 1) as i:
                phase0(i, False, False)
            phase0(NI - 1, False, True)

            def phase(g, prepare):
                with act.Fori(0, NI) as i:
                    n = g * NF + i * U
                    m = g * TG + TG + i
                    if prepare:
                        square(m, (g + 1) % XSLOTS, i, g + 1)
                    gelu(n, i * U, 0)
                    gelu(n + 1, i * U + 1, 1)
                    magnitude(n, i * U, 0)
                    gelu(n + 2, i * U + 2, 0)
                    magnitude(n + 1, i * U + 1, 1)
                    gelu(n + 3, i * U + 3, 1)
                    magnitude(n + 2, i * U + 2, 0)
                    if prepare:
                        high_half(m, (g + 1) % 2, i)
                    magnitude(n + 3, i * U + 3, 1)

            with act.Fori(1, G - 1) as g:
                phase(g, True)
            phase(G - 1, False)

            act.wait_ge(down_ready, TG * (G - 1))
            for j in range(1, NF, 2):
                act.wait_ge(hscaled, NF * (G - 1) + j + 1)
                act.activation(tile_of(h, j), tile_of(h, j), ACT.Copy, bias=ROUND).then_inc(hround, 1)
                act.wait_ge(hround, j // 2 + 1)
                act.activation(tile_of(q, j), tile_of(h, j), ACT.Copy, bias=-ROUND).then_inc(q_odd_ready, 1)

        @block.vector
        def _(dve):
            def row_scales(c, slot, count):
                dve.wait_ge(stage_loaded[slot], 32 * count)
                dve.tensor_reduce(wmax[:, :], stage[:, slot].rearrange("p j h d -> p (j h) d"), AX_X, ALU.max,
                                  apply_absolute_value=True).then_inc(wmax_ready, 1)
                dve.wait_ge(wmax_ready, c + 1)
                dve.tensor_scalar(wmax[:, :], wmax[:, :], TINY, None, ALU.max).then_inc(wclamped, 1)
                dve.wait_ge(wclamped, c + 1)
                dve.tensor_scalar(wpow[:, :].bitcast(I32), wmax[:, :].bitcast(I32), EXPONENT, None,
                                  ALU.bitwise_and).then_inc(wpow_ready, 1)
                dve.wait_ge(wpow_ready, c + 1)
                dve.tensor_scalar(winv[:, slot, :].bitcast(I32), wpow[:, :].bitcast(I32), EXPONENT, None,
                                  ALU.bitwise_xor).then_inc(wcomplement, 1)
                dve.wait_ge(wcomplement, c + 1)
                dve.tensor_scalar(winv[:, slot, :], winv[:, slot, :], W_UP, None, ALU.mult).then_inc(winv_ready, 1)

            def row_undo(c):
                dve.wait_ge(spow_ready, 4)
                dst = unscale[:, bass.ds(2 * c, 2), :].rearrange("p j h -> p (j h)")
                dve.tensor_scalar(dst, wpow[:, :], sundo[:, :], UNDO_W, ALU.mult, ALU.mult).then_inc(unscale_ready, 1)

            def weight_low(j, ps=down_ps):
                dve.wait_ge(whi_ready, 2 * j + 2)
                for half in range(2):
                    dst = wT[:, bass.ds(j * WT + half * KD * 2 * P, KD * 2 * P)]
                    dst = dst.rearrange("p (k a n) -> p k a n", k=KD, a=2)
                    src = ps[half].rearrange("p (k n) -> p k n", k=KD)
                    dve.tensor_tensor(dst[:, :, 1, :], src, dst[:, :, 0, :], ALU.subtract).then_inc(wlo_ready, 1)

            def normalise(m, slot, i):
                dve.wait_ge(rstd_ready, m + 1)
                dve.tensor_scalar(xn[:, :], x_tile(slot, i), rstd[:, :], None, ALU.mult).then_inc(xn_ready, 1)

            def scale_tile(m, ps=xT_ps, dst=hs):
                dve.wait_ge(xT_ready, m + 1)
                s = scaleT[:, bass.ds(m, 1), :].rearrange("p o k -> p (o k)").unsqueeze(2).to_broadcast([P, KD, P])
                dve.tensor_tensor(dst[:, :, :], ps.rearrange("p (k n) -> p k n", k=KD), s,
                                  ALU.mult).then_inc(hs_ready, 1)

            def low_half(m, parity, i, src=hs):
                dve.wait_ge(hi_ready, m + 1)
                def half(part):
                    v = hT[:, bass.ds(parity * 2 * HP + part * HP, HP)].rearrange("p (k n) -> p k n", k=KD)
                    return v[:, :, bass.ds(i * P, P)]
                dve.tensor_tensor(half(1), src[:, :, :], half(0), ALU.subtract).then_inc(lo_ready, 1)

            def glu_tile(n, j, b, reused=True):
                if reused:
                    dve.wait_ge(q_ready, n - NF + 1)
                dve.wait_ge(gelu_ready, n + 1)
                dve.wait_ge(val_ready, n + 1)
                dve.scalar_tensor_tensor(out=tile_of(h, j), in0=val_ps[b], scalar=unscale[:, bass.ds(j, 1), 0],
                                         in1=glu[:, b, :], op0=ALU.mult, op1=ALU.mult).then_inc(h_ready, 1)

            def max_tile(n, b, g):
                dve.wait_ge(abs_ready, n + 1)
                if not isinstance(n, int) or n > 0:
                    dve.wait_ge(max_ready, n)
                dve.wait_ge(runmax_zero, g + 1)
                dve.tensor_tensor(runmax[:, :], glu[:, b, :], runmax[:, :], ALU.max).then_inc(max_ready, 1)

            def quant_scale(n, j, g):
                dve.wait_ge(sbc_ready, TG * g + TG)
                dve.tensor_tensor(tile_of(h, j), tile_of(h, j), stat_ps, ALU.mult).then_inc(hscaled, 1)

            def quant_round(n, j):
                dve.wait_ge(hscaled, n + 1)
                dve.tensor_scalar(tile_of(q, j), tile_of(h, j), ROUND, ROUND, ALU.add,
                                  ALU.subtract).then_inc(q_ready, 1)

            def token_scales(g):
                dve.wait_ge(maxT_ready, TG * g + TG)
                dve.tensor_reduce(mtok[:, :], stat_ps.rearrange("p (i f) -> p i f", i=TG), AX_X,
                                  ALU.max).then_inc(mraw_ready, 1)
                dve.memset(runmax[:, :], 0.0).then_inc(runmax_zero, 1)
                dve.wait_ge(mraw_ready, g + 1)
                dve.tensor_scalar(mtok[:, :], mtok[:, :], CLIP, None, ALU.max).then_inc(mtok_ready, 1)
                dve.wait_ge(mtok_ready, g + 1)
                dve.reciprocal(minv[:, :], mtok[:, :]).then_inc(minv_ready, 1)
                dve.wait_ge(minv_ready, g + 1)
                dve.tensor_scalar(stok[:, :], minv[:, :], QMAX, None, ALU.mult).then_inc(stok_ready, 1)

            def output_scales(g):
                if not isinstance(g, int) or g > 0:
                    dve.wait_ge(y_ready, TG * g)
                dve.tensor_scalar(ctok[:, :], mtok[:, :], wmean127[:, :], None, ALU.mult).then_inc(ctok_ready, 1)

            def add_residual(m, ps, slot, i, g):
                dve.wait_ge(down_ready, m + 1)
                dve.wait_ge(ctok_ready, g + 1)
                xt = x_tile(slot, i)
                dve.scalar_tensor_tensor(out=xt, in0=ps, scalar=ctok[:, i:i + 1], in1=xt, op0=ALU.mult,
                                         op1=ALU.add).then_inc(y_ready, 1)

            dve.memset(runmax[:, :], 0.0).then_inc(runmax_zero, 1)

            dve.wait_ge(nwT_ready, KD + 1)
            dve.tensor_copy(nwT, xT_ps).then_inc(nwT_copied, 1)
            dve.tensor_copy(cndT, stat_ps[:, 0:NBATCH]).then_inc(nwT_copied, 1)
            dve.wait_ge(scale_mm, KD)
            dve.tensor_scalar(scaleT[:, :, :].rearrange("p b k -> p k b"),
                              down_ps[0][:, 0:KD * NBATCH].rearrange("p (k b) -> p k b", k=KD), 1.0, None,
                              ALU.add).then_inc(scale_one, 1)
            dve.wait_ge(scale_one, 1)
            flat = scaleT[:, :, :].rearrange("p b k -> p (b k)")
            dve.tensor_reduce(smax[:, :], flat, AX_X, ALU.max, apply_absolute_value=True).then_inc(smax_ready, 1)
            row_scales(0, 0, 1)
            dve.wait_ge(smax_reduced, 1)
            dve.tensor_scalar(smax[:, :], smax_all[:, :], TINY, None, ALU.max).then_inc(spow_ready, 1)
            dve.wait_ge(spow_ready, 1)
            dve.tensor_scalar(spow[:, :].bitcast(I32), smax[:, :].bitcast(I32), EXPONENT, None,
                              ALU.bitwise_and).then_inc(spow_ready, 1)
            dve.wait_ge(spow_ready, 2)
            dve.tensor_scalar(sinv[:, :].bitcast(I32), spow[:, :].bitcast(I32), EXPONENT, None,
                              ALU.bitwise_xor).then_inc(spow_ready, 1)
            dve.tensor_scalar(sundo[:, :], spow[:, :], UNDO_H, None, ALU.mult).then_inc(spow_ready, 1)
            dve.wait_ge(spow_ready, 4)
            dve.tensor_scalar(flat, flat, sinv[:, :], H_UP, ALU.mult, ALU.mult).then_inc(scale_ready, 1)
            row_undo(0)
            dve.wait_ge(scale_ready, 1)
            first = [hs4[:, i, :].rearrange("p (k n) -> p k n", k=KD) for i in range(TG)]
            for i in range(TG):
                scale_tile(i, last_ps[i], first[i])
            for i in range(TG):
                low_half(i, 0, i, first[i])
            weight_low(0)
            row_scales(1, 1, 1)
            row_undo(1)
            weight_low(1, [xT_ps, stat_ps])

            def weight_mean():
                dve.wait_ge(wsum_ready, 1)
                dve.tensor_scalar(wmean[:, :], stat_ps[:, 0:1], 1.0 / (D * FF), CLIP, ALU.mult,
                                  ALU.max).then_inc(wmean_ready, 1)
                dve.wait_ge(wmean_ready, 1)
                dve.reciprocal(wrecip[:, :], wmean[:, :]).then_inc(wrecip_ready, 1)
                dve.tensor_scalar(wmean127[:, :], wmean[:, :], 1.0 / QMAX, None, ALU.mult).then_inc(wmean_ready, 1)

            def clip_down(t):
                dve.wait_ge(raw_magic, t + 1)
                dve.tensor_scalar(vb[:, bass.ds(t, 1), :].rearrange("p o f -> p (o f)"), raw(t), ROUND, 1.0,
                                  ALU.subtract, ALU.min).then_inc(vb_ready, 1)

            def tern_chunks(k0, count):
                for k in range(k0, k0 + count):
                    dve.wait_ge(ternT_ready, k + 1)
                    dve.tensor_scalar(tern[:, k * D:(k + 1) * D], down_ps[k % 2].bitcast(BF16)[:, 0:D], -1.0, None,
                                      ALU.max).then_inc(tern_ready, 1)

            def phase0(i, first, last):
                n = i * U
                for u in range(U):
                    if not last and u % 2:
                        row_scales(2 * i + 2 + u // 2, u // 2, i + 2)
                        row_undo(2 * i + 2 + u // 2)
                    if last:
                        tern_chunks(2 * u, 4 if u == 3 else 2)
                    glu_tile(n + u, n + u, u % 2, False)
                    if u > 0:
                        max_tile(n + u - 1, (u - 1) % 2, 0)
                    if u == 0:
                        normalise(TG + i, 1, i)
                    if u == 2:
                        scale_tile(TG + i)
                    if first and u == 3:
                        dve.wait_ge(asum_ready, KD)
                        dve.tensor_reduce(asum1[:, :], asum[:, :], AX_X, ALU.add).then_inc(asum1_ready, 1)
                    if u == 3:
                        max_tile(n + u, u % 2, 0)
                    if not last or u < 2:
                        weight_low(n + u + 2)
                    if u == 3:
                        low_half(TG + i, 1, i)
                    if not first and not last and u in (1, 2):
                        clip_down(2 * i - 3 + u)

            phase0(0, True, False)
            weight_mean()
            with dve.Fori(1, NI - 1) as i:
                phase0(i, False, False)
            phase0(NI - 1, False, True)
            token_scales(0)
            tern_chunks(10, 6)
            dve.wait_ge(wmean_ready, 2)
            output_scales(0)

            def phase(g, prepare):
                with dve.Fori(0, NI) as i:
                    n = g * NF + i * U
                    m = g * TG + TG + i
                    for u in range(U):
                        j = i * U + u
                        quant_scale(n + u - NF, j, g - 1)
                        quant_round(n + u - NF, j)
                        glu_tile(n + u, j, u % 2)
                        if u > 0:
                            max_tile(n + u - 1, (u - 1) % 2, g)
                        if prepare and u == 0:
                            normalise(m, (g + 1) % XSLOTS, i)
                        if prepare and u == 2:
                            scale_tile(m)
                    max_tile(n + U - 1, 1, g)
                    if prepare:
                        low_half(m, (g + 1) % 2, i)
                for i in range(TG):
                    if i == 2:
                        token_scales(g)
                    if i == 3 and not prepare:
                        for j in range(3):
                            quant_scale(g * NF + j, j, g)
                        dve.wait_ge(down_ready, TG * g)
                        quant_round(g * NF, 0)
                    add_residual(g * TG - TG + i, down_ps[i % 2], (g - 1) % XSLOTS, i, g - 1)
                output_scales(g)

            with dve.Fori(1, G - 1) as g:
                phase(g, True)
            phase(G - 1, False)

            n = NF * (G - 1)
            quant_round(n + 2, 2)
            with dve.Fori(1, NF // 2 - 1) as jj:
                quant_scale(n + 2 * jj + 1, 2 * jj + 1, G - 1)
                quant_scale(n + 2 * jj + 2, 2 * jj + 2, G - 1)
                quant_round(n + 2 * jj + 2, 2 * jj + 2)
            quant_scale(n + NF - 1, NF - 1, G - 1)
            for i in range(TG):
                add_residual(TG * (G - 1) + i, last_ps[i], (G - 1) % XSLOTS, i, G - 1)

        @block.tensor
        def _(pe):
            def turn(dst, src, ident_ap):
                return pe.transpose(dst, src, ident_ap)

            def turn_first(i):
                pe.wait_ge(xn_ready, i + 1)
                for k in range(KD):
                    last = turn(last_ps[i][:, k * P:(k + 1) * P], xn4[:, i, k * P:(k + 1) * P], ident[:, :])
                last.then_inc(xT_ready, 1)

            def turn_x(m):
                pe.wait_ge(xn_ready, m + 1)
                pe.wait_ge(hs_ready, m)
                for k in range(KD):
                    last = turn(xT_ps[:, k * P:(k + 1) * P], xn[:, k * P:(k + 1) * P], ident[:, :])
                last.then_inc(xT_ready, 1)

            def turn_weights(j, pos, ps=down_ps):
                if isinstance(j, int) and j == 0:
                    pe.wait_ge(first_scaled, 2)
                else:
                    pe.wait_ge(wscaled, 2 * j + 2)
                if not isinstance(j, int) or j > 1:
                    pe.wait_ge(wlo_ready, 2 * j)
                for half in range(2):
                    for k in range(KD):
                        last = turn(ps[half][:, k * P:(k + 1) * P],
                                    stage[:, pos // 2, pos % 2, half, k * P:(k + 1) * P], ident[:, :])
                last.then_inc(wT_ready, 1)

            def up_half(j, half, ps, parity):
                n_mm = 3 * KD
                c = 0
                for k in range(KD):
                    for w_part, h_part in ((0, 0), (0, 1), (1, 0)):
                        rhs = hT[:, bass.ds(parity * 2 * HP + h_part * HP + k * NT, NT)]
                        last = pe.matmul(ps, weight(j, half, k, w_part), rhs, start=(c == 0), stop=(c == n_mm - 1))
                        c += 1
                return last

            def up_gate(n, j, b, parity):
                if not isinstance(n, int) or n > 1:
                    pe.wait_ge(gelu_ready, n - 1)
                up_half(j, 1, gate_ps[b], parity).then_inc(gate_ready, 1)

            def up_val(n, j, b, parity):
                if not isinstance(n, int) or n > 1:
                    pe.wait_ge(h_ready, n - 1)
                up_half(j, 0, val_ps[b], parity).then_inc(val_ready, 1)

            def turn_max(g):
                pe.wait_ge(max_ready, NF * g + NF)
                for i in range(TG):
                    turn(stat_ps[:, i * P:(i + 1) * P], runmax[:, i * P:(i + 1) * P],
                         ident[:, :]).then_inc(maxT_ready, 1)

            def spread_scales(g):
                pe.wait_ge(stok_ready, g + 1)
                for i in range(TG):
                    turn(stat_ps[:, i * P:(i + 1) * P], stok[:, i:i + 1].to_broadcast([P, P]),
                         ident[:, :]).then_inc(sbc_ready, 1)

            def down_mm(ps, k, i):
                return pe.matmul(ps, q[:, bass.ds(k * NT + i * P, P)], tern[:, bass.ds(k * D, D)],
                                 start=(isinstance(k, int) and k == 0), stop=(isinstance(k, int) and k == NF - 1))

            pe.wait_ge(consts_ready, 1)
            pe.wait_ge(nw_loaded, 32)
            for k in range(KD):
                turn(xT_ps[:, k * P:(k + 1) * P], nw[:, k, :], ident[:, :]).then_inc(nwT_ready, 1)
            turn(stat_ps[:, 0:NBATCH], cnd, ident[0:NBATCH, 0:NBATCH]).then_inc(nwT_ready, 1)
            pe.wait_ge(nwT_copied, 2)
            for k in range(KD):
                pe.matmul(down_ps[0][:, k * NBATCH:(k + 1) * NBATCH], nwT[:, k * P:(k + 1) * P], cndT,
                          start=True, stop=True).then_inc(scale_mm, 1)
            for i in range(TG):
                turn_first(i)
            pe.wait_ge(scale_one, 1)
            turn_weights(0, 0)
            turn_weights(1, 1, [xT_ps, stat_ps])

            def turn_down(k0, count):
                if k0 == 0:
                    pe.wait_ge(identb_ready, 1)
                    pe.wait_ge(vb_ready, KD)
                for k in range(k0, k0 + count):
                    if k >= 2:
                        pe.wait_ge(tern_ready, k - 1)
                    for t in range(KD):
                        last = turn(down_ps[k % 2].bitcast(BF16)[:, t * P:(t + 1) * P],
                                    vb[:, t, k * P:(k + 1) * P], identb[:, :])
                    last.then_inc(ternT_ready, 1)

            def phase0(i, last):
                n = i * U
                for u in range(U):
                    pe.wait_ge(wlo_ready, 2 * (n + u) + 2)
                    if last and u == 3:
                        turn_down(6, 2)
                    up_gate(n + u, n + u, u % 2, 0)
                    if last:
                        pe.wait_ge(wlo_ready, 2 * min(n + u + 2, NF))
                        turn_down(8 if u == 3 else 2 * u, 2)
                    up_val(n + u, n + u, u % 2, 0)
                    if last and u < 2:
                        pe.wait_ge(tern_ready, 2 * u + 2)
                    if not last or u < 2:
                        turn_weights(n + u + 2, (u + 2) % 4)
                    if u == 1:
                        turn_x(TG + i)

            pe.wait_ge(lo_ready, TG)
            phase0(0, False)
            pe.wait_ge(asum1_ready, 1)
            pe.matmul(stat_ps[:, 0:1], ones[:, :], asum1[:, :], start=True, stop=True).then_inc(wsum_ready, 1)
            with pe.Fori(1, NI - 1) as i:
                phase0(i, False)
            phase0(NI - 1, True)

            def up_step(g, i, prepare, first=False):
                n = g * NF + i * U
                pe.wait_ge(lo_ready, TG * g + TG)
                for u in range(U):
                    up_gate(n + u, i * U + u, u % 2, g % 2)
                    if first and u == 0:
                        turn_max(0)
                        turn_down(10, 2)
                    if first and u == 1:
                        turn_down(14, 2)
                    up_val(n + u, i * U + u, u % 2, g % 2)
                    if first and u == 0:
                        spread_scales(0)
                        turn_down(12, 2)
                    if prepare and u == 1:
                        turn_x(g * TG + TG + i)

            def down(g):
                pe.wait_ge(q_ready, NF * g + NF)
                pe.wait_ge(tern_ready, NF)
                for i in range(TG):
                    if i >= 2:
                        pe.wait_ge(y_ready, TG * g + i - 1)
                    for k in range(NF):
                        last = down_mm(down_ps[i % 2], k, i)
                    last.then_inc(down_ready, 1)
                    if i == 0:
                        turn_max(g + 1)
                    if i == 2:
                        spread_scales(g + 1)

            up_step(1, 0, True, True)
            with pe.Fori(1, NI) as i:
                up_step(1, i, True)
            down(0)
            with pe.Fori(2, G - 1) as g:
                with pe.Fori(0, NI) as i:
                    up_step(g, i, True)
                down(g - 1)
            with pe.Fori(0, NI) as i:
                up_step(G - 1, i, False)
            down(G - 2)

            for k in range(NF):
                if k % 2:
                    pe.wait_ge(q_odd_ready, k // 2 + 1)
                else:
                    pe.wait_ge(q_ready, NF * (G - 1) + k // 2 + 1)
                for i in range(TG):
                    last = down_mm(last_ps[i], k, i)
                    if k == NF - 1:
                        last.then_inc(down_ready, 1)


_INS = ["x", "cond_256", "L0_cond_norm_w", "L0_cond_up_w", "L0_cond_down_w"]
_OUTS = [((64, 128, 512), "float32")]


def kernel(**inputs):
    import numpy as _np
    import concourse.bacc as _bacc
    from concourse import mybir as _mybir
    from concourse.bass_utils import run_bass_kernel_spmd as _run

    nc = _bacc.Bacc("TRN2", target_bir_lowering=False, num_devices=1)
    arrays, args = {}, []
    for name in _INS:
        a = _np.ascontiguousarray(inputs[name])
        arrays[f"in_{name}_dram"] = a
        args.append(nc.dram_tensor(f"in_{name}_dram", a.shape, _mybir.dt.from_np(a.dtype), kind="ExternalInput").ap())
    for i, (shape, dtype) in enumerate(_OUTS):
        dt = _mybir.dt.from_np(_np.dtype(dtype))
        args.append(nc.dram_tensor(f"out_{i}_dram", shape, dt, kind="ExternalOutput").ap())
    bass_bitlinear_glu_kernel(nc, *args)
    r = _run(nc, [arrays], core_ids=[0])
    got = tuple(r.results[0][f"out_{i}_dram"] for i in range(len(_OUTS)))
    return got[0]
```
